# Optimizing a Trainium2 kernel written in Bass

```python
import numpy as np
import jax
import jax.numpy as jnp

def _softmax(x, axis=-1):
    return jax.nn.softmax(x, axis=axis)

def _gelu(x):
    return jax.nn.gelu(x, approximate=True)

def _silu(x):
    return jax.nn.silu(x)

def _sigmoid(x):
    return jax.nn.sigmoid(x)

def _layernorm(x, axis=-1, eps=1e-05):
    m = jnp.mean(x, axis=axis, keepdims=True)
    v = jnp.var(x, axis=axis, keepdims=True)
    return (x - m) / jnp.sqrt(v + eps)

def _scatter_add(tgt, idx, src, axis=0):
    return tgt.at[idx].add(src)

def _segment_sum(src, seg, n):
    return jax.ops.segment_sum(src, seg, n)
kernel_name = 'mk_macaron_d1_jaxref_r4_ea5878'

def setup_inputs(seed: int=0):
    np.random.seed(seed)
    _w = jnp.asarray

    def _L0_attn_setup():
        import jax, jax.numpy as jnp
        import numpy as np
        N_EMBD = 512
        EXPAND = 2
        D_INNER = N_EMBD * EXPAND
        D_STATE = 128
        N_HEADS = D_INNER // D_STATE
        HEAD_DIM = D_INNER // N_HEADS
        N_GROUPS = 1
        D_CONV = 4
        CHUNK = 64
        N_LAYERS = 48
        GS = N_GROUPS * D_STATE
        PROJ = 2 * D_INNER + N_HEADS + 2 * GS
        RMS_EPS = 1e-06

        def _ssd_scan(A, B, C, dt, x, chunk_size=CHUNK):
            batch, seq_len, n_heads, P = x.shape
            G, N = (B.shape[2], B.shape[3])
            Hg = n_heads // G
            Q = chunk_size
            pad_len = -seq_len % Q
            if pad_len:
                A = jnp.pad(A, ((0, 0), (0, pad_len), (0, 0)))
                B = jnp.pad(B, ((0, 0), (0, pad_len), (0, 0), (0, 0)))
                C = jnp.pad(C, ((0, 0), (0, pad_len), (0, 0), (0, 0)))
                dt = jnp.pad(dt, ((0, 0), (0, pad_len), (0, 0)))
                x = jnp.pad(x, ((0, 0), (0, pad_len), (0, 0), (0, 0)))
            T_pad = seq_len + pad_len
            n_chunks = T_pad // Q
            A_c = A.reshape(batch, n_chunks, Q, n_heads)
            B_c = B.reshape(batch, n_chunks, Q, G, N)
            C_c = C.reshape(batch, n_chunks, Q, G, N)
            dt_c = dt.reshape(batch, n_chunks, Q, n_heads)
            x_c = x.reshape(batch, n_chunks, Q, n_heads, P)
            log_a = A_c * dt_c
            cum_log_a = jnp.cumsum(log_a, axis=2)
            chunk_log_decay = cum_log_a[:, :, -1, :]
            log_diff = cum_log_a[:, :, :, None, :] - cum_log_a[:, :, None, :, :]
            causal = jnp.tril(jnp.ones((Q, Q), dtype=jnp.bool_))[None, None, :, :, None]
            L = jnp.exp(jnp.where(causal, log_diff, -jnp.inf))
            CB = jnp.einsum('bcign,bcjgn->bcijg', C_c, B_c)
            L_rs = L.reshape(batch, n_chunks, Q, Q, G, Hg)
            dt_rs = dt_c.reshape(batch, n_chunks, Q, G, Hg)
            x_rs = x_c.reshape(batch, n_chunks, Q, G, Hg, P)
            y_intra = jnp.einsum('bcijGH,bcijG,bcjGH,bcjGHp->bciGHp', L_rs, CB, dt_rs, x_rs)
            decay_to_end = jnp.exp(chunk_log_decay[:, :, None, :] - cum_log_a)
            decay_to_end_rs = decay_to_end.reshape(batch, n_chunks, Q, G, Hg)
            state_local = jnp.einsum('bcjGH,bcjGH,bcjGn,bcjGHp->bcGHnp', decay_to_end_rs, dt_rs, B_c, x_rs)
            chunk_decay = jnp.exp(chunk_log_decay).reshape(batch, n_chunks, G, Hg)

            def scan_op(left, right):
                d_l, s_l = left
                d_r, s_r = right
                return (d_l * d_r, d_r[..., None, None] * s_l + s_r)
            _, state_at_end = jax.lax.associative_scan(scan_op, (chunk_decay, state_local), axis=1)
            state_at_start = jnp.concatenate([jnp.zeros_like(state_at_end[:, :1]), state_at_end[:, :-1]], axis=1)
            decay_from_start = jnp.exp(cum_log_a).reshape(batch, n_chunks, Q, G, Hg)
            y_inter = jnp.einsum('bciGH,bciGn,bcGHnp->bciGHp', decay_from_start, C_c, state_at_start)
            y = (y_intra + y_inter).reshape(batch, T_pad, n_heads, P)
            if pad_len:
                y = y[:, :seq_len]
            return y
        key = jax.random.key(seed)
        ks = jax.random.split(key, 6)
        Bsz, T = (2, 512)
        x = jax.random.normal(ks[0], (Bsz, T, N_EMBD), jnp.float32)
        norm_scale = jnp.ones((N_EMBD,), jnp.float32)
        in_proj_w = 0.02 * jax.random.normal(ks[1], (N_EMBD, PROJ), jnp.float32)
        conv_weight = 0.02 * jax.random.normal(ks[2], (D_CONV, D_INNER), jnp.float32)
        conv_bias = jnp.zeros((D_INNER,), jnp.float32)
        A_log = jnp.log(jnp.arange(1, N_HEADS + 1, dtype=jnp.float32))
        dt_bias = 0.1 * jax.random.normal(ks[3], (N_HEADS,), jnp.float32)
        D = jnp.ones((D_INNER,), jnp.float32)
        out_proj_w = 0.02 / np.sqrt(2 * N_LAYERS) * jax.random.normal(ks[4], (D_INNER, N_EMBD), jnp.float32)
        return dict(x=x, norm_scale=norm_scale, in_proj_w=in_proj_w, conv_weight=conv_weight, conv_bias=conv_bias, A_log=A_log, dt_bias=dt_bias, D=D, out_proj_w=out_proj_w)
    _L0_attn_in = _L0_attn_setup()

    def _L0_ffn_setup():
        import jax, jax.numpy as jnp
        import numpy as np
        B, T, D = (1, 512, 512)
        E, K, F = (64, 4, 128)
        S, SF = (2, 128 * 4)
        CAP = 64

        def _moe_forward(x, router_w, router_bias, gate_w, up_w, down_w, sh_gate_w, sh_up_w, sh_down_w):
            b, t, d = x.shape
            flat = x.reshape(b * t, d)
            N = flat.shape[0]
            logits = flat @ router_w.T
            scores = jax.nn.softmax(logits, axis=-1)
            _, topk_idx = jax.lax.top_k(logits + router_bias, K)
            topk_w = jnp.take_along_axis(scores, topk_idx, axis=-1)
            topk_w = topk_w / topk_w.sum(axis=-1, keepdims=True)
            P = N * K
            e_flat = topk_idx.reshape(-1)
            t_flat = jnp.repeat(jnp.arange(N), K)
            w_flat = topk_w.reshape(-1)
            order = jnp.argsort(e_flat)
            e_s, t_s, w_s = (e_flat[order], t_flat[order], w_flat[order])
            counts = jnp.bincount(e_s, length=E)
            starts = jnp.concatenate([jnp.zeros((1,), counts.dtype), jnp.cumsum(counts)[:-1]])
            pos = jnp.arange(P) - starts[e_s]
            slot = jnp.where(pos < CAP, pos, CAP)
            tok_table = jnp.zeros((E, CAP + 1), jnp.int32).at[e_s, slot].set(t_s)[:, :CAP]
            w_table = jnp.zeros((E, CAP + 1), w_s.dtype).at[e_s, slot].set(w_s)[:, :CAP]
            xg = flat[tok_table]
            g = jnp.einsum('ecd,efd->ecf', xg, gate_w)
            u = jnp.einsum('ecd,efd->ecf', xg, up_w)
            y = jnp.einsum('ecf,edf->ecd', jax.nn.silu(g) * u, down_w)
            out = jnp.zeros_like(flat).at[tok_table.reshape(-1)].add((y * w_table[..., None]).reshape(-1, d))
            sg = jnp.einsum('nd,sfd->nsf', flat, sh_gate_w)
            su = jnp.einsum('nd,sfd->nsf', flat, sh_up_w)
            out = out + jnp.einsum('nsf,sdf->nd', jax.nn.silu(sg) * su, sh_down_w)
            return out.reshape(b, t, d)
        key = jax.random.key(seed)
        ks = jax.random.split(key, 9)
        s = 0.02
        return {'x': jax.random.normal(ks[0], (B, T, D), jnp.float32), 'router_w': jax.random.normal(ks[1], (E, D), jnp.float32) * s, 'router_bias': jnp.zeros((E,), jnp.float32), 'gate_w': jax.random.normal(ks[2], (E, F, D), jnp.float32) * s, 'up_w': jax.random.normal(ks[3], (E, F, D), jnp.float32) * s, 'down_w': jax.random.normal(ks[4], (E, D, F), jnp.float32) * s, 'sh_gate_w': jax.random.normal(ks[5], (S, SF, D), jnp.float32) * s, 'sh_up_w': jax.random.normal(ks[6], (S, SF, D), jnp.float32) * s, 'sh_down_w': jax.random.normal(ks[7], (S, D, SF), jnp.float32) * s}
    _L0_ffn_in = _L0_ffn_setup()
    _d = {'L0_attn_x': _L0_attn_in['x'], 'L0_attn_norm_scale': _L0_attn_in['norm_scale'], 'L0_attn_in_proj_w': _L0_attn_in['in_proj_w'], 'L0_attn_conv_weight': _L0_attn_in['conv_weight'], 'L0_attn_conv_bias': _L0_attn_in['conv_bias'], 'L0_attn_A_log': _L0_attn_in['A_log'], 'L0_attn_dt_bias': _L0_attn_in['dt_bias'], 'L0_attn_D': _L0_attn_in['D'], 'L0_attn_out_proj_w': _L0_attn_in['out_proj_w'], 'L0_ffn_router_w': _L0_ffn_in['router_w'], 'L0_ffn_router_bias': _L0_ffn_in['router_bias'], 'L0_ffn_gate_w': _L0_ffn_in['gate_w'], 'L0_ffn_up_w': _L0_ffn_in['up_w'], 'L0_ffn_down_w': _L0_ffn_in['down_w'], 'L0_ffn_sh_gate_w': _L0_ffn_in['sh_gate_w'], 'L0_ffn_sh_up_w': _L0_ffn_in['sh_up_w'], 'L0_ffn_sh_down_w': _L0_ffn_in['sh_down_w']}
    _x0 = _d['L0_attn_x']
    _d['L0_attn_x'] = jax.random.normal(jax.random.fold_in(jax.random.key(seed), 1), (2, 2048, 512), dtype=_x0.dtype)
    del _x0
    return _d

def reference(L0_attn_x, L0_attn_norm_scale, L0_attn_in_proj_w, L0_attn_conv_weight, L0_attn_conv_bias, L0_attn_A_log, L0_attn_dt_bias, L0_attn_D, L0_attn_out_proj_w, L0_ffn_router_w, L0_ffn_router_bias, L0_ffn_gate_w, L0_ffn_up_w, L0_ffn_down_w, L0_ffn_sh_gate_w, L0_ffn_sh_up_w, L0_ffn_sh_down_w):

    def _L0_attn_ref(x, norm_scale, in_proj_w, conv_weight, conv_bias, A_log, dt_bias, D, out_proj_w):
        import jax, jax.numpy as jnp
        import numpy as np
        N_EMBD = 512
        EXPAND = 2
        D_INNER = N_EMBD * EXPAND
        D_STATE = 128
        N_HEADS = D_INNER // D_STATE
        HEAD_DIM = D_INNER // N_HEADS
        N_GROUPS = 1
        D_CONV = 4
        CHUNK = 64
        N_LAYERS = 48
        GS = N_GROUPS * D_STATE
        PROJ = 2 * D_INNER + N_HEADS + 2 * GS
        RMS_EPS = 1e-06

        def _ssd_scan(A, B, C, dt, x, chunk_size=CHUNK):
            batch, seq_len, n_heads, P = x.shape
            G, N = (B.shape[2], B.shape[3])
            Hg = n_heads // G
            Q = chunk_size
            pad_len = -seq_len % Q
            if pad_len:
                A = jnp.pad(A, ((0, 0), (0, pad_len), (0, 0)))
                B = jnp.pad(B, ((0, 0), (0, pad_len), (0, 0), (0, 0)))
                C = jnp.pad(C, ((0, 0), (0, pad_len), (0, 0), (0, 0)))
                dt = jnp.pad(dt, ((0, 0), (0, pad_len), (0, 0)))
                x = jnp.pad(x, ((0, 0), (0, pad_len), (0, 0), (0, 0)))
            T_pad = seq_len + pad_len
            n_chunks = T_pad // Q
            A_c = A.reshape(batch, n_chunks, Q, n_heads)
            B_c = B.reshape(batch, n_chunks, Q, G, N)
            C_c = C.reshape(batch, n_chunks, Q, G, N)
            dt_c = dt.reshape(batch, n_chunks, Q, n_heads)
            x_c = x.reshape(batch, n_chunks, Q, n_heads, P)
            log_a = A_c * dt_c
            cum_log_a = jnp.cumsum(log_a, axis=2)
            chunk_log_decay = cum_log_a[:, :, -1, :]
            log_diff = cum_log_a[:, :, :, None, :] - cum_log_a[:, :, None, :, :]
            causal = jnp.tril(jnp.ones((Q, Q), dtype=jnp.bool_))[None, None, :, :, None]
            L = jnp.exp(jnp.where(causal, log_diff, -jnp.inf))
            CB = jnp.einsum('bcign,bcjgn->bcijg', C_c, B_c)
            L_rs = L.reshape(batch, n_chunks, Q, Q, G, Hg)
            dt_rs = dt_c.reshape(batch, n_chunks, Q, G, Hg)
            x_rs = x_c.reshape(batch, n_chunks, Q, G, Hg, P)
            y_intra = jnp.einsum('bcijGH,bcijG,bcjGH,bcjGHp->bciGHp', L_rs, CB, dt_rs, x_rs)
            decay_to_end = jnp.exp(chunk_log_decay[:, :, None, :] - cum_log_a)
            decay_to_end_rs = decay_to_end.reshape(batch, n_chunks, Q, G, Hg)
            state_local = jnp.einsum('bcjGH,bcjGH,bcjGn,bcjGHp->bcGHnp', decay_to_end_rs, dt_rs, B_c, x_rs)
            chunk_decay = jnp.exp(chunk_log_decay).reshape(batch, n_chunks, G, Hg)

            def scan_op(left, right):
                d_l, s_l = left
                d_r, s_r = right
                return (d_l * d_r, d_r[..., None, None] * s_l + s_r)
            _, state_at_end = jax.lax.associative_scan(scan_op, (chunk_decay, state_local), axis=1)
            state_at_start = jnp.concatenate([jnp.zeros_like(state_at_end[:, :1]), state_at_end[:, :-1]], axis=1)
            decay_from_start = jnp.exp(cum_log_a).reshape(batch, n_chunks, Q, G, Hg)
            y_inter = jnp.einsum('bciGH,bciGn,bcGHnp->bciGHp', decay_from_start, C_c, state_at_start)
            y = (y_intra + y_inter).reshape(batch, T_pad, n_heads, P)
            if pad_len:
                y = y[:, :seq_len]
            return y
        residual = x
        b, t = (x.shape[0], x.shape[1])
        h = x * jax.lax.rsqrt(jnp.mean(x * x, axis=-1, keepdims=True) + RMS_EPS) * norm_scale
        proj = h @ in_proj_w
        gate = proj[..., :D_INNER]
        ssm_in = proj[..., D_INNER:2 * D_INNER]
        dt_raw = proj[..., 2 * D_INNER:2 * D_INNER + N_HEADS]
        Bm = proj[..., 2 * D_INNER + N_HEADS:2 * D_INNER + N_HEADS + GS].reshape(b, t, N_GROUPS, D_STATE)
        Cm = proj[..., 2 * D_INNER + N_HEADS + GS:].reshape(b, t, N_GROUPS, D_STATE)
        xp = jnp.pad(ssm_in, ((0, 0), (D_CONV - 1, 0), (0, 0)))
        w_t = conv_weight.T[:, None, :]
        y = jax.lax.conv_general_dilated(jnp.transpose(xp, (0, 2, 1)), w_t, window_strides=(1,), padding='VALID', feature_group_count=D_INNER)
        ssm_in = jnp.transpose(y, (0, 2, 1)) + conv_bias
        ssm_in = jax.nn.silu(ssm_in)
        dt = jax.nn.softplus(dt_raw + dt_bias)
        A = -jnp.exp(A_log)
        A_f = jnp.broadcast_to(A[None, None, :], (b, t, N_HEADS))
        x_h = ssm_in.reshape(b, t, N_HEADS, HEAD_DIM)
        y_ssd = _ssd_scan(A_f, Bm, Cm, dt, x_h).reshape(b, t, D_INNER)
        y_ssd = y_ssd + D * ssm_in
        y_ssd = y_ssd * jax.nn.silu(gate)
        return residual + y_ssd @ out_proj_w

    def _L0_ffn_ref(x, router_w, router_bias, gate_w, up_w, down_w, sh_gate_w, sh_up_w, sh_down_w):
        import jax, jax.numpy as jnp
        import numpy as np
        B, T, D = (1, 512, 512)
        E, K, F = (64, 4, 128)
        S, SF = (2, 128 * 4)
        CAP = 64

        def _moe_forward(x, router_w, router_bias, gate_w, up_w, down_w, sh_gate_w, sh_up_w, sh_down_w):
            b, t, d = x.shape
            flat = x.reshape(b * t, d)
            N = flat.shape[0]
            logits = flat @ router_w.T
            scores = jax.nn.softmax(logits, axis=-1)
            _, topk_idx = jax.lax.top_k(logits + router_bias, K)
            topk_w = jnp.take_along_axis(scores, topk_idx, axis=-1)
            topk_w = topk_w / topk_w.sum(axis=-1, keepdims=True)
            P = N * K
            e_flat = topk_idx.reshape(-1)
            t_flat = jnp.repeat(jnp.arange(N), K)
            w_flat = topk_w.reshape(-1)
            order = jnp.argsort(e_flat)
            e_s, t_s, w_s = (e_flat[order], t_flat[order], w_flat[order])
            counts = jnp.bincount(e_s, length=E)
            starts = jnp.concatenate([jnp.zeros((1,), counts.dtype), jnp.cumsum(counts)[:-1]])
            pos = jnp.arange(P) - starts[e_s]
            slot = jnp.where(pos < CAP, pos, CAP)
            tok_table = jnp.zeros((E, CAP + 1), jnp.int32).at[e_s, slot].set(t_s)[:, :CAP]
            w_table = jnp.zeros((E, CAP + 1), w_s.dtype).at[e_s, slot].set(w_s)[:, :CAP]
            xg = flat[tok_table]
            g = jnp.einsum('ecd,efd->ecf', xg, gate_w)
            u = jnp.einsum('ecd,efd->ecf', xg, up_w)
            y = jnp.einsum('ecf,edf->ecd', jax.nn.silu(g) * u, down_w)
            out = jnp.zeros_like(flat).at[tok_table.reshape(-1)].add((y * w_table[..., None]).reshape(-1, d))
            sg = jnp.einsum('nd,sfd->nsf', flat, sh_gate_w)
            su = jnp.einsum('nd,sfd->nsf', flat, sh_up_w)
            out = out + jnp.einsum('nsf,sdf->nd', jax.nn.silu(sg) * su, sh_down_w)
            return out.reshape(b, t, d)
        return _moe_forward(x, router_w, router_bias, gate_w, up_w, down_w, sh_gate_w, sh_up_w, sh_down_w)
    x = L0_attn_x
    x = x + 0.5 * _L0_ffn_ref(_layernorm(x, axis=-1), L0_ffn_router_w, L0_ffn_router_bias, L0_ffn_gate_w, L0_ffn_up_w, L0_ffn_down_w, L0_ffn_sh_gate_w, L0_ffn_sh_up_w, L0_ffn_sh_down_w)
    x = x + _L0_attn_ref(_layernorm(x, axis=-1), L0_attn_norm_scale, L0_attn_in_proj_w, L0_attn_conv_weight, L0_attn_conv_bias, L0_attn_A_log, L0_attn_dt_bias, L0_attn_D, L0_attn_out_proj_w)
    x = x + 0.5 * _L0_ffn_ref(_layernorm(x, axis=-1), L0_ffn_router_w, L0_ffn_router_bias, L0_ffn_gate_w, L0_ffn_up_w, L0_ffn_down_w, L0_ffn_sh_gate_w, L0_ffn_sh_up_w, L0_ffn_sh_down_w)
    return x

_drawn_inputs = setup_inputs


def setup_inputs(seed=0):
    import zlib

    import numpy as np

    out = dict(_drawn_inputs(seed))
    spreads = {'L0_attn_norm_scale': (1.0, 0.2),
     'L0_attn_conv_bias': (0.0, 0.1),
     'L0_attn_D': (1.0, 0.2),
     'L0_ffn_router_bias': (0.0, 0.1)}
    factors = {}
    for name, (base, spread) in spreads.items():
        noise = np.random.default_rng([zlib.crc32(name.encode()), seed]).standard_normal(out[name].shape)
        drawn = base * np.exp(spread * noise) if base else spread * noise
        out[name] = jnp.asarray(drawn.astype(out[name].dtype))
    for name, factor in factors.items():
        out[name] = (out[name] * factor).astype(out[name].dtype)
    return out
```

```python
from contextlib import ExitStack

import concourse.bass as bass
from concourse import mybir

ALU = mybir.AluOpType
ACT = mybir.ActivationFunctionType
F32 = mybir.dt.float32
F32R = mybir.dt.float32r
BF16 = mybir.dt.bfloat16
U32 = mybir.dt.uint32
AX_X = mybir.AxisListType.X

P = 128
BATCH, SEQ, D = 2, 2048, 512
T = BATCH * SEQ
KD = D // P
E, K, F, CAP = 64, 4, 128, 64
SLOTS = E * CAP
ROW = D + 2 * K + 1
R_WEIGHT, R_SLOT, R_TOKEN = D, D + K, D + 2 * K
FS = 1024
CF = FS // P
TILES = T // P
LN_EPS, RMS_EPS = 1e-5, 1e-6

BT = 512
NB = T // BT
TB = BT // P
PIECE = 2048
SHW = 2 * KD * FS + CF * D
PIECES = SHW // PIECE

PAIRS = E // 2
EU = 4
EW = KD * 2 * F + D

DI, NH, DS, CONV = 1024, 8, 128, 4
HP = DI // NH
CI = DI // P
BM = 256
NM = T // BM
TM = BM // P
PROJ = 2 * DI + NH + 2 * DS


def last_split(ne, count, body):
    with ne.Fori(0, count - 1) as i:
        body(i)
    body(count - 1)


def ends_split(ne, count, body):
    body(0)
    with ne.Fori(1, count - 1) as i:
        body(i)
    body(count - 1)


def is_(n, value):
    return isinstance(n, int) and n == value


def wait(engine, sem, value):
    if not is_(value, 0):
        engine.wait_ge(sem, value)


def wait_apart(c, ne, *waits):
    waits = [(sem, value if isinstance(value, int) else ne.to_reg(value)) for sem, value in waits if not is_(value, 0)]
    ne.wait_ge(c.built, c.BUILT)
    for sem, value in waits:
        ne.wait_ge(sem, value)


class Names:
    pass


class Phase:

    def __init__(self, nc):
        self.nc, self.taken = nc, []

    def __call__(self, name):
        self.taken.append(self.nc.alloc_semaphore(name=name))
        return self.taken[-1]

    def __enter__(self):
        return self

    def __exit__(self, *failure):
        if failure[0] is None:
            self.nc.clear_and_free_semaphores(self.taken)
            self.nc.all_engine_barrier()


def make_constants(nc, c, s):
    built = c.built = s("constants_built")
    c.BUILT = 17
    with nc.Block() as block:
        @block.gpsimd
        def _(pool):
            g = nc.gpsimd
            g.memset(c.ones[:], 1.0).then_inc(built, 1)
            g.memset(c.ident[:], 0.0).then_inc(built, 1)
            g.memset(c.neg_half[:], -0.5).then_inc(built, 1)
            g.memset(c.keep[:], 1.0).then_inc(built, 1)
            g.memset(c.cut[:], 0.0).then_inc(built, 1)
            g.memset(c.fold[:], 0.0).then_inc(built, 1)
            pool.wait_ge(built, 6)
            g.memset(c.keep[:, NM // 2:NM // 2 + 1], 0.0).then_inc(built, 1)
            g.memset(c.cut[:, NM // 2:NM // 2 + 1], -1e30).then_inc(built, 1)
            g.affine_select(out=c.ident[:], in_=c.ident[:], compare_op=ALU.not_equal, fill=1.0, base=0,
                            pattern=[[-1, P]], channel_multiplier=1).then_inc(built, 1)
            g.affine_select(out=c.upto[:], in_=c.ones[:], compare_op=ALU.is_ge, fill=0.0, base=0,
                            pattern=[[1, P]], channel_multiplier=-1).then_inc(built, 1)
            g.affine_select(out=c.before[:], in_=c.ones[:], compare_op=ALU.is_ge, fill=0.0, base=-1,
                            pattern=[[1, P]], channel_multiplier=-1).then_inc(built, 1)
            g.affine_select(out=c.fold[:], in_=c.fold[:], compare_op=ALU.not_equal, fill=1.0, base=0,
                            pattern=[[-1, E]], channel_multiplier=1).then_inc(built, 1)
            pool.wait_ge(built, 12)
            g.affine_select(out=c.fold[:], in_=c.fold[:], compare_op=ALU.not_equal, fill=1.0, base=-E,
                            pattern=[[-1, E]], channel_multiplier=1).then_inc(built, 1)
            g.iota(c.token_no[:], pattern=[[P, TILES]], base=1, channel_multiplier=1,
                   allow_small_or_imprecise_dtypes=True).then_inc(built, 1)
            g.iota(c.slot_no[:], pattern=[[P, PAIRS]], base=0, channel_multiplier=1,
                   allow_small_or_imprecise_dtypes=True).then_inc(built, 1)
            g.iota(c.spare_row[:], pattern=[[0, 1]], base=T, channel_multiplier=1,
                   allow_small_or_imprecise_dtypes=True).then_inc(built, 1)
            g.tensor_copy(c.ones_bf[:], c.ones[:]).then_inc(built, 1)
            g.iota(c.expert_no[:], pattern=[[1, E]], base=0, channel_multiplier=0,
                   allow_small_or_imprecise_dtypes=True).then_inc(built, 1)
            pool.wait_ge(built, c.BUILT)


def route_and_shared(nc, tag, c, s, src, acc, xg, shw, routw, routb, first_token, clear_slots):
    src_b = src[0:T, :].rearrange("(b j p) d -> b p j d", p=P, j=TB)
    acc_b = acc[0:T, :].rearrange("(b j p) d -> b p j d", p=P, j=TB)
    with ExitStack() as ctx:
        def sb(name, shape, dt=F32):
            return ctx.enter_context(nc.sbuf_tensor(f"{name}_{tag}", shape, dt))

        def ps(name, shape, dt=F32):
            return ctx.enter_context(nc.psum_tensor(f"{name}_{tag}", shape, dt))

        def sem(name):
            return s(f"{name}_{tag}")

        w_hi, w_lo = sb("w_hi", [P, SHW], F32R), sb("w_lo", [P, SHW], F32R)
        r_both = sb("r_both", [P, KD, 2, E], F32R)
        r_raw = sb("r_raw", [P, KD * E])
        rbias = sb("rbias", [P, E])
        x = [sb(f"x{u}", [P, TB, D]) for u in range(2)]
        h = [sb(f"h{u}", [P, TB, ROW]) for u in range(2)]
        logit_t = sb("logit_t", [P, BT])
        ht_hi, ht_lo = sb("ht_hi", [P, KD, BT], F32R), sb("ht_lo", [P, KD, BT], F32R)
        act_hi, act_lo = sb("act_hi", [P, CF, BT], F32R), sb("act_lo", [P, CF, BT], F32R)
        silu = sb("silu", [P, 2, BT])
        prod = sb("prod", [P, 2, BT])
        stats = sb("stats", [P, TB, 6])
        mv = sb("mv", [P, TB, 2])
        var_eps, rstd = sb("var_eps", [P, TB]), sb("rstd", [P, TB])
        biased = sb("biased", [P, TB, E])
        expo = sb("expo", [P, TB, E])
        top_logit = sb("top_logit", [P, TB])
        best = sb("best", [P, TB, 8])
        best_no = sb("best_no", [P, TB, 8], U32)
        choice = sb("choice", [P, TB, K])
        onehot = sb("onehot", [P, TB, K, E])
        picked = sb("picked", [P, TB, K, E])
        chosen = sb("chosen", [P, TB, E], BF16)
        chosen_before = sb("chosen_before", [P, E], BF16)
        chosen_sum = sb("chosen_sum", [P, E])
        place = sb("place", [P, TB, E])
        slot = sb("slot", [P, TB * K])
        weight = sb("weight", [P, TB, K])
        wsum = sb("wsum", [P, TB])
        slot_now = [sb(f"slot_now{u}", [P, TB * K], U32) for u in range(2)]
        zeros = sb("zeros", [P, ROW])
        stage = [x[1], h[1]]

        p_gate, p_up, p_out = ps("p_gate", [P, 2, BT]), ps("p_up", [P, 2, BT]), ps("p_out", [P, 2, D])
        p_t = ps("p_t", [P, 2, BT])
        p_logit = p_t[:, 1, 0:TB * E].rearrange("p (j e) -> p j e", e=E)
        p_count = p_t[:, 0, 0:TB * E].rearrange("p (j e) -> p j e", e=E)

        piece_loaded = [sem(f"piece_loaded{i}") for i in range(2)]
        small_loaded, w_hi_done, w_lo_done = sem("small_loaded"), sem("w_hi_done"), sem("w_lo_done")
        r_split = sem("r_split")
        zeros_set, slots_cleared = sem("zeros_set"), sem("slots_cleared")
        x_loaded, x_stored = [sem(f"x_loaded{u}") for u in range(2)], [sem(f"x_stored{u}") for u in range(2)]
        var_ready, rstd_ready, h_ready = sem("var_ready"), sem("rstd_ready"), sem("h_ready")
        t_full, ht_hi_ready, ht_ready = sem("t_full"), sem("ht_hi_ready"), sem("ht_ready")
        logit_t_full, logit_t_ready = sem("logit_t_full"), sem("logit_t_ready")
        logits_full, shifted_ready, expo_ready = sem("logits_full"), sem("shifted_ready"), sem("expo_ready")
        chosen_ready, count_full, slot_ready = sem("chosen_ready"), sem("count_full"), sem("slot_ready")
        count_read = sem("count_read")
        rows_sent = [sem(f"rows_sent{u}") for u in range(2)]
        gate_full, up_full, silu_ready = sem("gate_full"), sem("up_full"), sem("silu_ready")
        prod_ready, act_hi_ready, act_ready = sem("prod_ready"), sem("act_hi_ready"), sem("act_ready")
        out_full, acc_ready = sem("out_full"), sem("acc_ready")
        dve_step = sem("dve_step")

        wgu = lambda w: w[:, 0:2 * KD * FS].rearrange("p (n g k f) -> p n g k f", n=CF, g=2, k=KD)
        wd = lambda w: w[:, 2 * KD * FS:SHW].rearrange("p (c d) -> p c d", c=CF)
        r_view = r_raw[:, :].rearrange("p (k e) -> p k e", k=KD)
        flat = lambda t: t[:, :, :].rearrange("p j d -> p (j d)")[:, 0:PIECE]

        with nc.Block() as block:
            @block.sync
            def _(sp):
                sp.dma_start(x[0][:], src_b[0]).then_inc(x_loaded[0], 16)
                sp.dma_start(r_raw[:], routw).then_inc(small_loaded, 16)
                sp.dma_start(rbias[:], routb.to_broadcast([P, E])).then_inc(small_loaded, 16)
                for i in range(PIECES):
                    if i >= 2:
                        sp.wait_ge(w_lo_done, i - 1)
                    sp.dma_start(flat(stage[i % 2]), shw[:, i * PIECE:(i + 1) * PIECE]).then_inc(
                        piece_loaded[i % 2], 16)
                sp.wait_ge(w_lo_done, PIECES - 1)
                sp.dma_start(x[1][:], src_b[1]).then_inc(x_loaded[1], 16)

                def store_and_load(b, it, u, more):
                    sp.wait_ge(acc_ready, b * TB + TB)
                    sp.dma_start(acc_b[b], x[u][:]).then_inc(x_stored[u], 16)
                    if more:
                        sp.wait_ge(x_stored[u], it * 16 + 16)
                        sp.dma_start(x[u][:], src_b[b + 2]).then_inc(x_loaded[u], 16)

                def pair(it):
                    for u in range(2):
                        store_and_load(2 * it + u, it, u, not is_(it, NB // 2 - 1))
                last_split(nc.sync, NB // 2, pair)
                for u in range(2):
                    sp.wait_ge(x_stored[u], 16 * (NB // 2))

            @block.gpsimd
            def _(pool):
                g = nc.gpsimd
                def inv_std(b):
                    pool.wait_ge(var_ready, b + 1)
                    g.tensor_tensor(rstd[:], var_eps[:], c.neg_half[:, 0:TB], ALU.pow).then_inc(rstd_ready, 1)

                g.memset(zeros[:], 0.0).then_inc(zeros_set, 1)
                inv_std(0)
                pool.wait_ge(zeros_set, 1)
                pool.dma_start(acc[T:T + P, :], zeros[:, 0:D]).then_inc(slots_cleared, 16)
                if clear_slots:
                    n = SLOTS // P
                    pool.wait_ge(w_lo_done, PIECES - 1)
                    pool.dma_start(xg.rearrange("(p a) d -> p (a d)", p=P).rearrange("p (n m) -> p n m", n=n),
                                   zeros[:, :].unsqueeze(1).to_broadcast([P, n, ROW])).then_inc(slots_cleared, 16)

                def send_rows(b, u):
                    wait_apart(c, g, (slots_cleared, 32 if clear_slots else 16), (slot_ready, b + 1))
                    for j in range(TB):
                        for k in range(K):
                            g.indirect_dma_start(
                                out=xg, out_offset=bass.IndirectOffsetOnAxis(
                                    ap=slot_now[u][:, j * K + k:j * K + k + 1], axis=0),
                                in_=h[u][:, j, :], in_offset=None, bounds_check=SLOTS - 1,
                                oob_is_err=False).then_inc(rows_sent[u], 16)

                def pair(it):
                    for u in range(2):
                        b = 2 * it + u
                        if not is_(b, NB - 1):
                            inv_std(b + 1)
                        send_rows(b, u)
                ends_split(g, NB // 2, pair)
                for u in range(2):
                    pool.wait_ge(rows_sent[u], 16 * TB * K * (NB // 2))

            @block.scalar
            def _(act):
                a = nc.scalar

                def split(i):
                    act.wait_ge(piece_loaded[i % 2], 16 * (i // 2 + 1))
                    a.activation(w_hi[:, i * PIECE:(i + 1) * PIECE], flat(stage[i % 2]), ACT.Copy).then_inc(w_hi_done, 1)

                def front(b):
                    for k in range(KD):
                        act.wait_ge(t_full, b * KD + k + 1)
                        a.activation(ht_hi[:, k, :], p_t[:, k % 2, :], ACT.Copy).then_inc(ht_hi_ready, 1)

                def exponents(b):
                    act.wait_ge(shifted_ready, b + 1)
                    a.activation(expo[:], expo[:], ACT.Exp).then_inc(expo_ready, 1)

                def turn_logits(b):
                    act.wait_ge(logit_t_full, b + 1)
                    a.activation(logit_t[:], p_t[:, 0, :], ACT.Copy).then_inc(logit_t_ready, 1)

                def shared(b):
                    for n in range(CF):
                        if is_(b, 0) and n + 1 < PIECES:
                            split(n + 1)
                        act.wait_ge(gate_full, b * CF + n + 1)
                        wait(act, prod_ready, b * CF + max(n - 1, 0))
                        a.activation(silu[:, n % 2, :], p_gate[:, n % 2, :], ACT.Silu).then_inc(silu_ready, 1)
                        act.wait_ge(prod_ready, b * CF + n + 1)
                        a.activation(act_hi[:, n, :], prod[:, n % 2, :], ACT.Copy).then_inc(act_hi_ready, 1)

                act.wait_ge(small_loaded, 32)
                a.activation(r_both[:, :, 0, :], r_view, ACT.Copy).then_inc(r_split, 1)
                split(0)
                front(0)
                turn_logits(0)
                exponents(0)

                def pair(it):
                    for u in range(2):
                        b = 2 * it + u
                        shared(b)
                        if not is_(b, NB - 1):
                            front(b + 1)
                            turn_logits(b + 1)
                            exponents(b + 1)
                ends_split(a, NB // 2, pair)

            @block.tensor
            def _(pe):
                t = nc.tensor

                def three(out, l_hi, l_lo, r_hi_, r_lo_, first, last):
                    t.matmul(out, l_hi, r_hi_, start=first, stop=False)
                    t.matmul(out, l_hi, r_lo_, start=False, stop=False)
                    return t.matmul(out, l_lo, r_hi_, start=False, stop=last)

                def turn(b, u, k):
                    pe.wait_ge(h_ready, b * TB + TB)
                    if k >= 2:
                        pe.wait_ge(ht_ready, b * KD + k - 1)
                    elif k == 0:
                        wait(pe, count_read, b)
                    else:
                        wait(pe, shifted_ready, b)
                    for j in range(TB):
                        mm = t.matmul(p_t[:, k % 2, j * P:(j + 1) * P], h[u][:, j, k * P:(k + 1) * P],
                                      c.ident[:], is_transpose=True, start=True, stop=True)
                    mm.then_inc(t_full, 1)

                def logits_turned(b):
                    pe.wait_ge(ht_ready, b * KD + KD)
                    for k in range(KD):
                        for rhs in (ht_hi, ht_lo):
                            mm = t.matmul(p_t[:, 0, :], r_both[:, k, :, :].rearrange("p a e -> p (a e)"), rhs[:, k, :],
                                          start=(k == 0 and rhs is ht_hi), stop=(k == KD - 1 and rhs is ht_lo))
                    mm.then_inc(logit_t_full, 1)

                def logits(b):
                    pe.wait_ge(logit_t_ready, b + 1)
                    for j in range(TB):
                        mm = t.matmul(p_logit[:, j, :], logit_t[:, j * P:(j + 1) * P], c.fold[:], start=True, stop=True)
                    mm.then_inc(logits_full, 1)

                def counts(b):
                    pe.wait_ge(chosen_ready, b + 1)
                    for j in range(TB):
                        t.matmul(p_count[:, j, :], c.ones_bf[:], chosen_before[:], start=True, stop=False)
                        for i in range(j):
                            t.matmul(p_count[:, j, :], c.ones_bf[:], chosen[:, i, :], start=False, stop=False)
                        mm = t.matmul(p_count[:, j, :], c.before[:], chosen[:, j, :], start=False, stop=True)
                    mm.then_inc(count_full, 1)

                def gate_up(b, n):
                    if is_(b, 0):
                        pe.wait_ge(w_lo_done, n // 2 + 1)
                    for i, (out, full, free) in enumerate(((p_gate, gate_full, silu_ready), (p_up, up_full, prod_ready))):
                        wait(pe, free, b * CF + max(n - 1, 0))
                        for k in range(KD):
                            mm = three(out[:, n % 2, :], wgu(w_hi)[:, n, i, k, :], wgu(w_lo)[:, n, i, k, :],
                                       ht_hi[:, k, :], ht_lo[:, k, :], k == 0, k == KD - 1)
                        mm.then_inc(full, 1)

                def down(b, j):
                    if is_(b, 0) and j == 0:
                        pe.wait_ge(w_lo_done, PIECES)
                    wait(pe, acc_ready, b * TB + max(j - 1, 0))
                    tok = slice(j * P, (j + 1) * P)
                    for n in range(CF):
                        if j == 0:
                            pe.wait_ge(act_ready, b * CF + n + 1)
                        mm = three(p_out[:, j % 2, :], act_hi[:, n, tok], act_lo[:, n, tok],
                                   wd(w_hi)[:, n, :], wd(w_lo)[:, n, :], n == 0, n == CF - 1)
                    mm.then_inc(out_full, 1)

                for k in range(KD):
                    turn(0, 0, k)
                pe.wait_ge(r_split, 2)
                logits_turned(0)
                logits(0)

                def pair(it):
                    for u in range(2):
                        b = 2 * it + u
                        more = not is_(b, NB - 1)
                        for n in range(CF):
                            gate_up(b, n)
                            if n == 1:
                                counts(b)
                        if more:
                            turn(b + 1, 1 - u, 0)
                            turn(b + 1, 1 - u, 1)
                        down(b, 0)
                        if more:
                            turn(b + 1, 1 - u, 2)
                            turn(b + 1, 1 - u, 3)
                        down(b, 1)
                        if more:
                            logits_turned(b + 1)
                        down(b, 2)
                        if more:
                            logits(b + 1)
                        down(b, 3)
                ends_split(t, NB // 2, pair)

            @block.vector
            def _(dve):
                v = nc.vector
                steps = [0, 0]

                def link(ins):
                    steps[1] += 1
                    ins.then_inc(dve_step, 1)
                    dve.wait_ge(dve_step, steps[0] + steps[1])

                def link_apart(ins):
                    steps[1] += 1
                    ins.then_inc(dve_step, 1)
                    wait_apart(c, v, (dve_step, steps[0] + steps[1]))

                def split(i):
                    dve.wait_ge(w_hi_done, i + 1)
                    cols = slice(i * PIECE, (i + 1) * PIECE)
                    v.tensor_tensor(w_lo[:, cols], flat(stage[i % 2]), w_hi[:, cols].bitcast(F32),
                                    ALU.subtract).then_inc(w_lo_done, 1)

                v.memset(chosen_before[:], 0.0)

                def norm_stats(b, it, u):
                    dve.wait_ge(x_loaded[u], it * 16 + 16)
                    for j in range(TB):
                        ins = v.bn_stats(stats[:, j, :], x[u][:, j, :])
                    link_apart(ins)
                    for j in range(TB):
                        ins = v.bn_aggr(mv[:, j, :], stats[:, j, :])
                    link(ins)
                    v.tensor_scalar(var_eps[:], mv[:, :, 1], LN_EPS, None, ALU.add).then_inc(var_ready, 1)

                def norm_apply(b, it, u):
                    dve.wait_ge(rstd_ready, b + 1)
                    wait(dve, rows_sent[u], it * (16 * TB * K))
                    for j in range(TB):
                        v.tensor_scalar(h[u][:, j, 0:D], x[u][:, j, :], mv[:, j, 0:1], rstd[:, j:j + 1],
                                        ALU.subtract, ALU.mult).then_inc(h_ready, 1)
                    v.tensor_scalar(h[u][:, :, R_TOKEN], c.token_no[:, bass.ds(b * TB, TB)], float(first_token), None,
                                    ALU.add)

                def turned(b, k):
                    dve.wait_ge(ht_hi_ready, b * KD + k + 1)
                    v.tensor_tensor(ht_lo[:, k, :], p_t[:, k % 2, :], ht_hi[:, k, :].bitcast(F32),
                                    ALU.subtract).then_inc(ht_ready, 1)

                def choose(b):
                    dve.wait_ge(logits_full, b + 1)
                    v.tensor_tensor(biased[:], p_logit, rbias[:].unsqueeze(1).to_broadcast([P, TB, E]), ALU.add)
                    link(v.tensor_reduce(top_logit[:], p_logit, AX_X, ALU.max))
                    v.tensor_tensor(expo[:], p_logit, top_logit[:].unsqueeze(2).to_broadcast([P, TB, E]),
                                    ALU.subtract).then_inc(shifted_ready, 1)
                    for j in range(TB):
                        ins = v.max(best[:, j, :], biased[:, j, :])
                    link_apart(ins)
                    for j in range(TB):
                        ins = v.max_index(best_no[:, j, :], best[:, j, :], biased[:, j, :])
                    link(ins)
                    link(v.tensor_copy(choice[:], best_no[:, :, 0:K]))
                    link(v.tensor_tensor(
                        onehot[:].rearrange("p j k e -> p (j k) e"),
                        c.expert_no[:].unsqueeze(1).to_broadcast([P, TB * K, E]),
                        choice[:].rearrange("p j k -> p (j k)").unsqueeze(2).to_broadcast([P, TB * K, E]),
                        ALU.is_equal))
                    with nc.allow_low_precision(reason="a sum of zeros and at most one 1"):
                        v.tensor_reduce(chosen[:], onehot[:].rearrange("p j k e -> p j e k"), AX_X,
                                        ALU.add).then_inc(chosen_ready, 1)

                def assign(b, u):
                    dve.wait_ge(count_full, b + 1)
                    link(v.tensor_scalar(place[:], p_count, float(CAP), float(2 * SLOTS), ALU.is_ge, ALU.mult))
                    v.tensor_tensor(place[:], p_count, place[:], ALU.add).then_inc(count_read, 1)
                    dve.wait_ge(count_read, b + 1)
                    pk = picked[:]
                    oh = onehot[:]
                    link(v.tensor_tensor(pk, oh, place[:].unsqueeze(2).to_broadcast([P, TB, K, E]), ALU.mult))
                    link(v.tensor_reduce(slot[:].rearrange("p (j k) -> p j k", k=K), pk, AX_X, ALU.add))
                    ch = choice[:].rearrange("p j k -> p (j k)")
                    link(v.scalar_tensor_tensor(slot[:], ch, float(CAP), slot[:], ALU.mult, ALU.add))
                    v.tensor_copy(h[u][:, :, R_SLOT:R_SLOT + K], slot[:].rearrange("p (j k) -> p j k", k=K))
                    v.tensor_copy(slot_now[u][:], slot[:])
                    dve.wait_ge(expo_ready, b + 1)
                    link(v.tensor_tensor(pk, oh, expo[:].unsqueeze(2).to_broadcast([P, TB, K, E]), ALU.mult))
                    link(v.tensor_reduce(weight[:], pk, AX_X, ALU.add))
                    link(v.tensor_reduce(wsum[:], weight[:], AX_X, ALU.add))
                    link(v.reciprocal(wsum[:], wsum[:]))
                    v.tensor_tensor(h[u][:, :, R_WEIGHT:R_WEIGHT + K], weight[:],
                                    wsum[:].unsqueeze(2).to_broadcast([P, TB, K]), ALU.mult).then_inc(slot_ready, 1)
                    link(v.tensor_reduce(chosen_sum[:], chosen[:].rearrange("p j e -> p e j"), AX_X, ALU.add))
                    link(v.tensor_tensor(chosen_before[:], chosen_before[:], chosen_sum[:], ALU.add))

                def chunk(b, n):
                    dve.wait_ge(silu_ready, b * CF + n + 1)
                    dve.wait_ge(up_full, b * CF + n + 1)
                    v.tensor_tensor(prod[:, n % 2, :], silu[:, n % 2, :], p_up[:, n % 2, :],
                                    ALU.mult).then_inc(prod_ready, 1)
                    dve.wait_ge(prod_ready, b * CF + n + 1)
                    dve.wait_ge(act_hi_ready, b * CF + n + 1)
                    v.tensor_tensor(act_lo[:, n, :], prod[:, n % 2, :], act_hi[:, n, :].bitcast(F32),
                                    ALU.subtract).then_inc(act_ready, 1)

                def finish(b, u, j):
                    dve.wait_ge(out_full, b * TB + j + 1)
                    v.scalar_tensor_tensor(x[u][:, j, :], p_out[:, j % 2, :], 0.5, x[u][:, j, :],
                                           ALU.mult, ALU.add).then_inc(acc_ready, 1)

                norm_stats(0, 0, 0)
                norm_apply(0, 0, 0)
                dve.wait_ge(r_split, 1)
                v.tensor_tensor(r_both[:, :, 1, :], r_view, r_both[:, :, 0, :].bitcast(F32),
                                ALU.subtract).then_inc(r_split, 1)
                for k in range(KD):
                    turned(0, k)
                split(0)
                choose(0)
                HEAD = steps[1]

                def pair(it):
                    for u in range(2):
                        b = 2 * it + u
                        nb, nit, nu = b + 1, (it if u == 0 else it + 1), 1 - u
                        more, first = not is_(b, NB - 1), is_(b, 0)
                        stats_at, apply_at = (4, 6) if first else (0, 1)
                        steps[0], steps[1] = b * BODY + HEAD, 0
                        for n in range(CF):
                            if first and n + 1 < PIECES:
                                split(n + 1)
                            chunk(b, n)
                            if more and n == stats_at:
                                norm_stats(nb, nit, nu)
                            if more and n == apply_at:
                                norm_apply(nb, nit, nu)
                            if n == 2:
                                assign(b, u)
                        if more:
                            turned(nb, 0)
                            turned(nb, 1)
                        finish(b, u, 0)
                        if more:
                            turned(nb, 2)
                            turned(nb, 3)
                        finish(b, u, 1)
                        finish(b, u, 2)
                        if more:
                            choose(nb)
                        finish(b, u, 3)
                        if more:
                            assert steps[1] == BODY, steps
                BODY = HEAD + 10
                ends_split(v, NB // 2, pair)


def experts(nc, tag, c, s, xg, ew, acc, first_token):
    xg_q = xg.rearrange("(q p) d -> q p d", p=P)
    SECOND = slice(CAP, P)
    with ExitStack() as ctx:
        def sb(name, shape, dt=F32):
            return ctx.enter_context(nc.sbuf_tensor(f"{name}_{tag}", shape, dt))

        def ps(name, shape, dt=F32):
            return ctx.enter_context(nc.psum_tensor(f"{name}_{tag}", shape, dt))

        def sem(name):
            return s(f"{name}_{tag}")

        rows = [sb(f"rows{u}", [P, ROW]) for u in range(EU)]
        w = [sb(f"ew{u}", [P, 2, EW]) for u in range(EU)]
        xt = sb("xt", [P, 2, KD, P])
        silu, prod, pt = sb("esilu", [P, 2, F]), sb("eprod", [P, 2, F]), sb("ept", [P, 2, P + CAP])
        y = [sb(f"ey{u}", [P, D]) for u in range(EU)]
        turner = [sb(f"turner{u}", [P, P + CAP]) for u in range(2)]
        knows = []
        for u in range(EU):
            b = Names()
            b.taken, b.past, b.hit, b.half_w = sb(f"taken{u}", [P, 1]), sb(f"past{u}", [P, 1]), sb(f"hit{u}", [P, K]), sb(f"half_w{u}", [P, 1])
            b.row, b.twice, b.to_spare = sb(f"row{u}", [P, 1]), sb(f"twice{u}", [P, 1]), sb(f"to_spare{u}", [P, 1])
            b.row_no = sb(f"row_no{u}", [P, 1], U32)
            knows.append(b)
        p_xt, p_gu, p_pt, p_y = ps("p_xt", [P, D]), ps("p_gu", [P, 2, D]), ps("p_pt", [P, D]), ps("p_y", [P, 2, D])
        p_rows = ps("p_rows", [P, D])
        rows_loaded = [sem(f"rows_loaded{u}") for u in range(EU)]
        w_loaded = [sem(f"w_loaded{u}") for u in range(EU)]
        xt_full, xt_ready, gu_full, silu_ready = sem("xt_full"), sem("xt_ready"), sem("gu_full"), sem("esilu_ready")
        prod_ready, pt_full, pt_ready = sem("eprod_ready"), sem("pt_full"), sem("pt_ready")
        y_full, y_ready, added = sem("y_full"), sem("y_ready"), sem("added")
        know_step, weight_ready, rows_full, cross_ready = sem("know_step"), sem("weight_ready"), sem("rows_full"), sem("cross_ready")
        turner_set, row_no_ready = sem("turner_set"), sem("row_no_ready")
        N = PAIRS // EU

        def below(q, n):
            return isinstance(q, int) and q < n

        with nc.Block() as block:
            @block.sync
            def _(sp):
                def group(it):
                    for u in range(EU):
                        q = it * EU + u
                        if not below(q, EU):
                            sp.wait_ge(xt_full, q - EU + 1)
                            sp.wait_ge(weight_ready, q - EU + 1)
                        sp.dma_start(rows[u][:], xg_q[q]).then_inc(rows_loaded[u], 16)
                        if not below(q, EU):
                            sp.wait_ge(y_full, q - EU + 1)
                        sp.dma_start(w[u][:], ew[q]).then_inc(w_loaded[u], 16)
                ends_split(nc.sync, N, group)

            @block.gpsimd
            def _(pool):
                g = nc.gpsimd
                for u in range(2):
                    g.memset(turner[u][:], 0.0).then_inc(turner_set, 1)
                pool.wait_ge(turner_set, 2)
                for u in range(2):
                    g.tensor_copy(turner[u][:, 0:P], c.ident[:]).then_inc(turner_set, 1)

                def group(it):
                    for u in range(EU):
                        q = it * EU + u
                        wait_apart(c, g, (y_ready, q + 1), (row_no_ready, 2 * q + 2), (added, q * 16))
                        g.indirect_dma_start(
                            out=acc, out_offset=bass.IndirectOffsetOnAxis(ap=knows[u].row_no[:, 0:1], axis=0),
                            in_=y[u][:], in_offset=None, bounds_check=T + P - 1, oob_is_err=True,
                            compute_op=ALU.add).then_inc(added, 16)
                ends_split(g, N, group)
                pool.wait_ge(added, PAIRS * 16)

            @block.tensor
            def _(pe):
                t = nc.tensor

                def turn_rows(q, it, u):
                    pe.wait_ge(rows_loaded[u], it * 16 + 16)
                    wait(pe, xt_ready, q)
                    for k in range(KD):
                        mm = t.matmul(p_xt[:, k * P:(k + 1) * P], rows[u][:, k * P:(k + 1) * P],
                                      c.ident[:], is_transpose=True, start=True, stop=True)
                    mm.then_inc(xt_full, 1)

                def gate_up(q, it, u):
                    pe.wait_ge(xt_ready, q + 1)
                    pe.wait_ge(w_loaded[u], it * 16 + 16)
                    if not below(q, 2):
                        pe.wait_ge(prod_ready, q - 1)
                    for e in range(2):
                        for k in range(KD):
                            mm = t.matmul(p_gu[e * CAP:(e + 1) * CAP, u % 2, 0:2 * F],
                                          xt[:, u % 2, k, e * CAP:(e + 1) * CAP],
                                          w[u][:, e, k * 2 * F:(k + 1) * 2 * F], start=(k == 0), stop=(k == KD - 1))
                    mm.then_inc(gu_full, 1)

                def spread_rows(q, u):
                    pe.wait_ge(weight_ready, q + 1)
                    wait(pe, cross_ready, q)
                    t.matmul(p_rows[:, 0:P], knows[u].row[:, 0:1].to_broadcast([P, P]), c.ident[:],
                             start=True, stop=True).then_inc(rows_full, 1)

                def turn_prod(q, u):
                    pe.wait_ge(prod_ready, q + 1)
                    pe.wait_ge(cross_ready, q + 1)
                    wait(pe, pt_ready, q)
                    t.matmul(p_pt[:, 0:P + CAP], prod[:, u % 2, :], turner[u % 2][:],
                             start=True, stop=True).then_inc(pt_full, 1)

                def down(q, u):
                    pe.wait_ge(pt_ready, q + 1)
                    if not below(q, 2):
                        pe.wait_ge(y_ready, q - 1)
                    bank = p_y[:, u % 2, :]
                    first, second = w[u][:, 0, KD * 2 * F:EW], w[u][:, 1, KD * 2 * F:EW]
                    t.matmul(bank[0:CAP, :], pt[:, u % 2, 0:CAP], first, start=True, stop=False)
                    t.matmul(bank[SECOND, :], pt[:, u % 2, SECOND], second, start=True, stop=True)
                    t.matmul(bank[0:CAP, :], pt[:, u % 2, P:P + CAP], second, start=False,
                             stop=True).then_inc(y_full, 1)

                turn_rows(0, 0, 0)
                pe.wait_ge(turner_set, 4)
                spread_rows(0, 0)

                def group(it):
                    for u in range(EU):
                        q = it * EU + u
                        last = is_(q, PAIRS - 1)
                        if not last:
                            turn_rows(q + 1, it if u < EU - 1 else it + 1, (u + 1) % EU)
                        gate_up(q, it, u)
                        if not is_(q, 0):
                            down(q - 1, (u - 1) % EU)
                        if not last:
                            spread_rows(q + 1, (u + 1) % EU)
                        turn_prod(q, u)
                ends_split(t, N, group)
                down(PAIRS - 1, EU - 1)

            @block.scalar
            def _(act):
                a = nc.scalar

                def out(q, u):
                    act.wait_ge(y_full, q + 1)
                    if not below(q, EU):
                        act.wait_ge(added, (q - EU + 1) * 16)
                    a.activation(y[u][:], p_y[:, u % 2, :], ACT.Copy).then_inc(y_ready, 1)

                def group(it):
                    for u in range(EU):
                        q = it * EU + u
                        act.wait_ge(gu_full, q + 1)
                        if not below(q, 2):
                            act.wait_ge(prod_ready, q - 1)
                        a.activation(silu[:, u % 2, :], p_gu[:, u % 2, 0:F], ACT.Silu).then_inc(silu_ready, 1)
                        if not is_(q, 0):
                            out(q - 1, (u - 1) % EU)
                ends_split(a, N, group)
                out(PAIRS - 1, EU - 1)

            @block.vector
            def _(dve):
                v = nc.vector
                KNOW = 4

                def linked(q):
                    steps = [q * KNOW]

                    def link(ins):
                        ins.then_inc(know_step, 1)
                        steps[0] += 1
                        dve.wait_ge(know_step, steps[0])
                    return link, steps

                def rows_out(q, u):
                    dve.wait_ge(xt_full, q + 1)
                    v.tensor_copy(xt[:, u % 2, :, :], p_xt[:, :].rearrange("p (k t) -> p k t", k=KD)).then_inc(xt_ready, 1)

                def know(q, it, u):
                    link, steps = linked(q)
                    b, token = knows[u], rows[u][:, R_TOKEN:R_TOKEN + 1]
                    dve.wait_ge(rows_loaded[u], it * 16 + 16)
                    if not below(q, EU):
                        dve.wait_ge(row_no_ready, (q - EU + 1) * 2)
                        dve.wait_ge(prod_ready, q - EU + 1)
                        dve.wait_ge(rows_full, q - EU + 1)
                    v.tensor_scalar(b.taken[:], token, float(first_token + 1), None, ALU.is_ge)
                    v.scalar_tensor_tensor(b.past[:], token, float(first_token + 1), c.spare_row[:],
                                           ALU.subtract, ALU.subtract)
                    link(v.scalar_tensor_tensor(b.hit[:], rows[u][:, R_SLOT:R_SLOT + K], c.slot_no[:, bass.ds(q, 1)],
                                                rows[u][:, R_WEIGHT:R_WEIGHT + K], ALU.is_equal, ALU.mult))
                    v.scalar_tensor_tensor(b.row[:], b.past[:], b.taken[:], c.spare_row[:], ALU.mult, ALU.add)
                    link(v.tensor_reduce(b.half_w[:], b.hit[:], AX_X, ALU.add))
                    v.scalar_tensor_tensor(b.half_w[:], b.half_w[:], 0.5, b.taken[:], ALU.mult,
                                           ALU.mult).then_inc(weight_ready, 1)

                def join(q, u):
                    link, steps = linked(q)
                    steps[0] += 2
                    b, cross = knows[u], turner[u % 2][SECOND, P:P + CAP]
                    if below(q, 2):
                        dve.wait_ge(turner_set, 4)
                    dve.wait_ge(rows_full, q + 1)
                    v.tensor_scalar(cross, p_rows[SECOND, 0:CAP], b.row[SECOND, :], None, ALU.is_equal).then_inc(cross_ready, 1)
                    link(v.tensor_tensor(b.to_spare[SECOND, :], c.spare_row[SECOND, :], b.row[SECOND, :], ALU.subtract))
                    dve.wait_ge(cross_ready, q + 1)
                    link(v.tensor_reduce(b.twice[SECOND, :], cross, AX_X, ALU.add))
                    if not below(q, EU):
                        dve.wait_ge(added, (q - EU + 1) * 16)
                    v.tensor_copy(b.row_no[0:CAP, :], b.row[0:CAP, :]).then_inc(row_no_ready, 1)
                    v.scalar_tensor_tensor(b.row_no[SECOND, :], b.to_spare[SECOND, :], b.twice[SECOND, :],
                                           b.row[SECOND, :], ALU.mult, ALU.add).then_inc(row_no_ready, 1)

                rows_out(0, 0)
                know(0, 0, 0)
                join(0, 0)

                def group(it):
                    for u in range(EU):
                        q = it * EU + u
                        nq, nit, nu = q + 1, (it if u < EU - 1 else it + 1), (u + 1) % EU
                        last = is_(q, PAIRS - 1)
                        if not last:
                            rows_out(nq, nu)
                            know(nq, nit, nu)
                        dve.wait_ge(silu_ready, q + 1)
                        dve.wait_ge(weight_ready, q + 1)
                        v.scalar_tensor_tensor(prod[:, u % 2, :], silu[:, u % 2, :], knows[u].half_w[:, 0:1],
                                               p_gu[:, u % 2, F:2 * F], ALU.mult, ALU.mult).then_inc(prod_ready, 1)
                        if not last:
                            join(nq, nu)
                        dve.wait_ge(pt_full, q + 1)
                        v.tensor_copy(pt[:, u % 2, :], p_pt[:, 0:P + CAP]).then_inc(pt_ready, 1)
                ends_split(v, N, group)


def mamba(nc, c, s, src, dst, ins):
    src_b = src[0:T, :].rearrange("(b j p) d -> b p j d", p=P, j=TM)
    dst_b = dst.rearrange("(b j p) d -> b p j d", p=P, j=TM)
    HALF = PROJ // 2
    OUTC = 1024
    IN_PIECES, OUT_PIECES = 2 * KD, CI * D // OUTC
    N_PIECES = IN_PIECES + OUT_PIECES
    HALO = CONV - 1
    GATE0, SSM0, DT0, B0, C0 = 0, DI, 2 * DI, 2 * DI + NH, 2 * DI + NH + DS
    JOBS = 6 + 2 * CI
    J_DT, J_C, J_B, J_TOK, J_CUM, J_CB = 0, 1, 2, 3, 6, 8
    J_SSM = [4, 5, 7, 9, 10, 11, 12, 13]
    J_GATE = list(range(14, 22))

    with ExitStack() as ctx:
        def sb(name, shape, dt=F32):
            return ctx.enter_context(nc.sbuf_tensor(f"m_{name}", shape, dt))

        def ps(name, shape, dt=F32):
            return ctx.enter_context(nc.psum_tensor(f"m_{name}", shape, dt))

        def sem(name):
            return s(f"m_{name}")

        wi_hi, wi_lo = sb("wi_hi", [P, KD, PROJ], F32R), sb("wi_lo", [P, KD, PROJ], F32R)
        wo_hi, wo_lo = sb("wo_hi", [P, CI, D], F32R), sb("wo_lo", [P, CI, D], F32R)
        nscale, convw, convb, dskip = sb("nscale", [P, KD]), sb("convw", [P, CI, CONV]), sb("convb", [P, CI]), sb("dskip", [P, CI])
        dtb, a_neg = sb("dtb", [P, NH]), sb("a_neg", [P, NH])
        x = [sb(f"x{u}", [P, TM, D]) for u in range(2)]
        h = sb("h", [P, TM, D])
        ht_hi, ht_lo = sb("ht_hi", [P, KD, BM], F32R), sb("ht_lo", [P, KD, BM], F32R)
        stats, mv = sb("stats", [P, TM, 6]), sb("mv", [P, TM, 2])
        var2, inv2 = sb("var2", [P, 2, TM]), sb("inv2", [P, 2, TM])
        one_inv, mean_inv = sb("one_inv", [P, TM]), sb("mean_inv", [P, TM])
        ssm = sb("ssm", [P, CI, HALO + BM])
        xt = sb("xt", [P, CI, BM])
        gate = sb("gate", [P, CI, BM])
        dtt, bt, ct = sb("dtt", [NH, BM]), sb("bt", [P, BM]), sb("ct", [P, BM])
        tok = sb("tok", [P, TM * P + TM * NH])
        btok = tok[:, 0:TM * P].rearrange("p (j n) -> p j n", j=TM)
        dtraw = tok[:, TM * P:]
        dtv, nabs, dt, la = sb("dtv", [P, TM, NH]), sb("nabs", [P, TM, NH]), sb("dt", [P, TM, NH]), sb("la", [P, TM, NH])
        cum = sb("cum", [P, 2, TM, NH])
        to_end, etot = sb("to_end", [P, TM, NH]), sb("etot", [P, TM, NH])
        cb = sb("cb", [P, TM, P])
        decay = [sb(f"decay{j}", [P, NH, P]) for j in range(TM)]
        cdec = [sb(f"cdec{j}", [P, NH, P]) for j in range(TM)]
        xdt = [sb(f"xdt{j}", [P, NH, HP]) for j in range(TM)]
        xs = sb("xs", [P, NH, HP])
        state, state_dec = sb("state", [P, NH, HP]), sb("state_dec", [P, NH, HP])
        y_hi, y_lo = sb("y_hi", [P, CI, P], F32R), sb("y_lo", [P, CI, P], F32R)

        p_ab = ps("p_ab", [P, 2, 512])
        p_x, p_cr, p_y = ps("p_x", [P, 2, 512]), ps("p_cr", [P, 2, 512]), ps("p_y", [P, 2, 512])
        heads = lambda t: t[:, :, :].rearrange("p b (h q) -> p (b h) q", q=P)

        flat = lambda t: t[:, :, :].rearrange("p a b -> p (a b)")
        stage = [flat(xt), flat(gate), flat(ssm)]

        piece_loaded = [sem(f"piece_loaded{i}") for i in range(3)]
        small_loaded, w_hi_done, w_lo_done = sem("small_loaded"), sem("w_hi_done"), sem("w_lo_done")
        a_exp, set_up = sem("a_exp"), sem("set_up")
        x_loaded, x_stored = [sem(f"x_loaded{u}") for u in range(2)], [sem(f"x_stored{u}") for u in range(2)]
        var_ready, inv_ready, h_ready = sem("var_ready"), sem("inv_ready"), sem("h_ready")
        t_full, ht_hi_ready, ht_ready = sem("t_full"), sem("ht_hi_ready"), sem("ht_ready")
        ab_full, ab_free = sem("ab_full"), sem("ab_free")
        nabs_ready, soft_ready, la_ready = sem("nabs_ready"), sem("soft_ready"), sem("la_ready")
        soft_exp = sem("soft_exp")
        to_end_ready, ends_ready, etot_ready = sem("to_end_ready"), sem("ends_ready"), sem("etot_ready")
        cr_full, cdec_exp, cdec_ready = sem("cr_full"), sem("cdec_exp"), sem("cdec_ready")
        diff_ready, decay_exp, decay_ready = sem("diff_ready"), sem("decay_exp"), sem("decay_ready")
        tap_ready, conv_ready, halo_ready, xt_ready, gate_ready = (
            sem("tap_ready"), sem("conv_ready"), sem("halo_ready"), sem("xt_ready"), sem("gate_ready"))
        xtr_full, xdt_ready, xs_ready = sem("xtr_full"), sem("xdt_ready"), sem("xs_ready")
        y_full, y_read, y_gated, y_hi_ready, y_ready = (
            sem("y_full"), sem("y_read"), sem("y_gated"), sem("y_hi_ready"), sem("y_ready"))
        s_full, state_dec_ready, state_ready = sem("s_full"), sem("state_dec_ready"), sem("state_ready")
        out_full, out_ready = sem("out_full"), sem("out_ready")
        dve_step = sem("dve_step")

        def piece(i):
            if i < IN_PIECES:
                k, cols = i // 2, slice((i % 2) * HALF, (i % 2 + 1) * HALF)
                return ins["winp"][:, k * PROJ + (i % 2) * HALF:k * PROJ + (i % 2 + 1) * HALF], HALF, \
                    wi_hi[:, k, cols], wi_lo[:, k, cols], nscale[:, k:k + 1]
            m = i - IN_PIECES
            rows = slice(m * (OUTC // D), (m + 1) * (OUTC // D))
            return ins["wout"][:, m * OUTC:(m + 1) * OUTC], OUTC, flat(wo_hi)[:, m * OUTC:(m + 1) * OUTC], \
                flat(wo_lo)[:, m * OUTC:(m + 1) * OUTC], None

        def pairs(body):
            return lambda it: [body(2 * it + u, it, u) for u in range(2)]

        with nc.Block() as block:
            @block.sync
            def _(sp):
                for name, part in (("nscale", nscale[:]), ("convw", flat(convw)), ("convb", convb[:]),
                                   ("dskip", dskip[:])):
                    sp.dma_start(part, ins[name]).then_inc(small_loaded, 16)
                sp.dma_start(dtb[:], ins["dtb"].to_broadcast([P, NH])).then_inc(small_loaded, 16)
                sp.dma_start(a_neg[:], ins["alog"].to_broadcast([P, NH])).then_inc(small_loaded, 16)
                for i in range(N_PIECES):
                    if i >= 3:
                        sp.wait_ge(w_lo_done, i - 2)
                    w, cols, _, _, _ = piece(i)
                    sp.dma_start(stage[i % 3][:, 0:cols], w).then_inc(piece_loaded[i % 3], 16)
                    if i == 2:
                        for b in range(2):
                            sp.dma_start(x[b][:], src_b[b]).then_inc(x_loaded[b], 16)

                def store_and_load(n, it, u):
                    sp.wait_ge(out_ready, n * TM + TM)
                    sp.dma_start(dst_b[n], x[u][:]).then_inc(x_stored[u], 16)
                    if not (isinstance(n, int) and n >= NM - 2):
                        sp.wait_ge(x_stored[u], it * 16 + 16)
                        sp.dma_start(x[u][:], src_b[n + 2]).then_inc(x_loaded[u], 16)
                last_split(nc.sync, NM // 2, pairs(store_and_load))
                for u in range(2):
                    sp.wait_ge(x_stored[u], 16 * (NM // 2))

            @block.gpsimd
            def _(pool):
                g = nc.gpsimd

                def inv_std(n):
                    pool.wait_ge(var_ready, n + 1)
                    g.tensor_tensor(inv2[:], var2[:], c.neg_half[:, 0:2 * TM].rearrange("p (a j) -> p a j", a=2),
                                    ALU.pow).then_inc(inv_ready, 1)

                def block_(n, it, u):
                    for j in range(TM):
                        pool.wait_ge(cdec_exp, n * TM + j + 1)
                        g.tensor_tensor(cdec[j][:], cdec[j][:],
                                        ct[:, j * P:(j + 1) * P].unsqueeze(1).to_broadcast([P, NH, P]),
                                        ALU.mult).then_inc(cdec_ready, 1)
                    if not is_(n, NM - 1):
                        inv_std(n + 1)

                    def decay_state(j):
                        pool.wait_ge(etot_ready, n * TM + j + 1)
                        pool.wait_ge(state_ready, n * TM + j + 1)
                        g.tensor_tensor(state_dec[:], state[:], etot[:, j, :].unsqueeze(2).to_broadcast([P, NH, HP]),
                                        ALU.mult).then_inc(state_dec_ready, 1)

                    def decay_inputs(j):
                        wait(pool, s_full, n * TM + j)
                        pool.wait_ge(ends_ready, n + 1)
                        pool.wait_ge(xdt_ready, n * TM + j + 1)
                        g.tensor_tensor(xs[:], xdt[j][:], to_end[:, j, :].unsqueeze(2).to_broadcast([P, NH, HP]),
                                        ALU.mult).then_inc(xs_ready, 1)

                    decay_state(0)
                    decay_inputs(0)
                    decay_inputs(1)
                    decay_state(1)
                inv_std(0)
                ends_split(g, NM // 2, pairs(block_))

            @block.scalar
            def _(act):
                a = nc.scalar
                act.wait_ge(small_loaded, 96)
                a.activation(a_neg[:], a_neg[:], ACT.Exp).then_inc(a_exp, 1)
                for i in range(N_PIECES):
                    act.wait_ge(piece_loaded[i % 3], 16 * (i // 3 + 1))
                    _, cols, hi, _, scale = piece(i)
                    a.activation(hi, stage[i % 3][:, 0:cols], ACT.Identity if scale is not None else ACT.Copy,
                                 **({"scale": scale} if scale is not None else {})).then_inc(w_hi_done, 1)

                def turned(n):
                    for r in range(2):
                        act.wait_ge(t_full, n * 2 + r + 1)
                        a.activation(ht_hi[:, 2 * r:2 * r + 2, :], p_cr[:, r, :].rearrange("p (k t) -> p k t", k=2),
                                     ACT.Copy).then_inc(ht_hi_ready, 1)

                def copy_job(n, job, out, rows=P):
                    act.wait_ge(ab_full, n * JOBS + job + 1)
                    cols = out.free_size()
                    a.activation(out, p_ab[0:rows, job % 2, 0:cols] if len(out.shape) == 2 else
                                 p_ab[0:rows, job % 2, 0:cols].rearrange("p (j q) -> p j q", j=out.shape[1]),
                                 ACT.Copy).then_inc(ab_free, 1)

                def head(n):
                    copy_job(n, J_DT, dtt[:, :], NH)
                    wait(act, cdec_ready, n * TM)
                    copy_job(n, J_C, ct[:, :])
                    copy_job(n, J_B, bt[:, :])

                def block_(n, it, u):
                    wait(act, s_full, n * TM)
                    copy_job(n, J_TOK, tok[:, :])
                    act.wait_ge(nabs_ready, n + 1)
                    a.activation(nabs[:], nabs[:], ACT.Exp).then_inc(soft_exp, 1)
                    act.wait_ge(soft_exp, n + 1)
                    a.activation(nabs[:], nabs[:], ACT.Ln, bias=c.ones[:, 0:1]).then_inc(soft_ready, 1)

                    def ssm_job(m):
                        act.wait_ge(ab_full, n * JOBS + J_SSM[m] + 1)
                        if m == 0:
                            act.wait_ge(halo_ready, n + 1)
                            wait(act, y_ready, n * TM)
                        a.activation(xt[:, m, :], p_ab[:, J_SSM[m] % 2, 0:BM], ACT.Identity,
                                     bias=convb[:, m:m + 1], scale=convw[:, m, HALO:CONV]).then_inc(tap_ready, 1)
                        a.activation(ssm[:, m, HALO:], p_ab[:, J_SSM[m] % 2, 0:BM], ACT.Copy).then_inc(ab_free, 1)

                    ssm_job(0)
                    ssm_job(1)
                    wait(act, diff_ready, n * (TM * NH))
                    copy_job(n, J_CUM, cum[:, :, :, :].rearrange("p a j h -> p (a j h)"))
                    wait_apart(c, a, (ab_free, n * JOBS + J_CUM + 1), (state_dec_ready, n * TM))
                    a.activation(etot[:, 0, :], cum[:, 1, 0, :], ACT.Exp, bias=c.cut[:, bass.ds(n, 1)]).then_inc(etot_ready, 1)
                    a.activation(etot[:, 1, :], cum[:, 1, 1, :], ACT.Exp).then_inc(etot_ready, 1)
                    act.wait_ge(to_end_ready, n + 1)
                    a.activation(to_end[:], to_end[:], ACT.Exp).then_inc(ends_ready, 1)
                    ssm_job(2)
                    wait(act, decay_ready, n * TM)
                    copy_job(n, J_CB, cb[:, :, :])

                    def carried(j):
                        wait_apart(c, a, (cr_full, n * TM + j + 1), (y_full, n * TM))
                        bias = {"bias": c.cut[:, bass.ds(n, 1)]} if j == 0 else {}
                        a.activation(cdec[j][:], heads(p_cr), ACT.Exp, **bias).then_inc(cdec_exp, 1)

                    def within(j):
                        act.wait_ge(diff_ready, (n * TM + j) * NH + NH)
                        a.activation(decay[j][:], decay[j][:], ACT.Exp).then_inc(decay_exp, 1)

                    def silu_half(i):
                        act.wait_ge(conv_ready, n * CI + (i + 1) * CI // 2)
                        part = xt[:, i * CI // 2:(i + 1) * CI // 2, :]
                        a.activation(part, part, ACT.Silu).then_inc(xt_ready, 1)

                    def gate_job(m):
                        if m == 0:
                            wait(act, y_gated, n * TM)
                        copy_job(n, J_GATE[m], gate[:, m, :])

                    carried(0)
                    ssm_job(3)
                    within(0)
                    ssm_job(4)
                    ssm_job(5)
                    carried(1)
                    ssm_job(6)
                    within(1)
                    ssm_job(7)
                    silu_half(0)
                    for m in range(3):
                        gate_job(m)
                    silu_half(1)
                    for m in range(3, CI):
                        gate_job(m)
                    act.wait_ge(ab_free, n * JOBS + J_GATE[7] + 1)
                    a.activation(gate[:], gate[:], ACT.Silu).then_inc(gate_ready, 1)
                    if not is_(n, NM - 1):
                        turned(n + 1)
                        head(n + 1)
                    for j in range(TM):
                        act.wait_ge(y_gated, n * TM + j + 1)
                        wait(act, out_full, n * TM + j)
                        a.activation(y_hi[:], xt[:, :, j * P:(j + 1) * P], ACT.Copy).then_inc(y_hi_ready, 1)
                turned(0)
                head(0)
                ends_split(a, NM // 2, pairs(block_))

            @block.tensor
            def _(pe):
                t = nc.tensor

                def three(out, l_hi, l_lo, r_hi_, r_lo_, first, last):
                    t.matmul(out, l_hi, r_hi_, start=first, stop=False)
                    t.matmul(out, l_hi, r_lo_, start=False, stop=False)
                    return t.matmul(out, l_lo, r_hi_, start=False, stop=last)

                def turn(n):
                    pe.wait_ge(h_ready, n * TM + TM)
                    wait(pe, diff_ready, n * (TM * NH))
                    for k in range(KD):
                        for j in range(TM):
                            mm = t.matmul(p_cr[:, k // 2, (k % 2) * BM + j * P:(k % 2) * BM + (j + 1) * P],
                                          h[:, j, k * P:(k + 1) * P], c.ident[:], is_transpose=True,
                                          start=True, stop=True)
                        if k % 2:
                            mm.then_inc(t_full, 1)

                def ab(n, job):
                    pe.wait_ge(ab_free, n * JOBS + max(job - 1, 0))
                    return p_ab[:, job % 2, :]

                def project(n, job, col, width=P):
                    out = ab(n, job)[0:width, 0:BM]
                    for k in range(KD):
                        mm = three(out, wi_hi[:, k, col:col + width], wi_lo[:, k, col:col + width],
                                   ht_hi[:, k, :], ht_lo[:, k, :], k == 0, k == KD - 1)
                    mm.then_inc(ab_full, 1)

                def to_tokens(n):
                    pe.wait_ge(ab_free, n * JOBS + J_B + 1)
                    out = ab(n, J_TOK)
                    for j in range(TM):
                        t.matmul(out[:, j * P:(j + 1) * P], bt[:, j * P:(j + 1) * P], c.ident[:],
                                 is_transpose=True, start=True, stop=True)
                    for j in range(TM):
                        at = TM * P + j * NH
                        mm = t.matmul(out[:, at:at + NH], dtt[:, j * P:(j + 1) * P], c.ident[0:NH, 0:NH],
                                      is_transpose=True, start=True, stop=True)
                    mm.then_inc(ab_full, 1)

                def cumulate(n):
                    pe.wait_ge(la_ready, n + 1)
                    out = ab(n, J_CUM)
                    for i, m in enumerate((c.upto, c.ones)):
                        mm = t.matmul(out[:, i * TM * NH:(i + 1) * TM * NH], m[:],
                                      la[:, :, :].rearrange("p j h -> p (j h)"), start=True, stop=True)
                    mm.then_inc(ab_full, 1)

                def b_by_c(n):
                    out = ab(n, J_CB)
                    for j in range(TM):
                        tokens = slice(j * P, (j + 1) * P)
                        mm = t.matmul(out[:, tokens], bt[:, tokens], ct[:, tokens], start=True, stop=True)
                    mm.then_inc(ab_full, 1)

                def spread(n, j):
                    if j == 0:
                        pe.wait_ge(state_ready, n * TM + 1)
                    else:
                        pe.wait_ge(diff_ready, (n * TM + j) * NH)
                    for hd in range(NH):
                        mm = t.matmul(heads(p_cr)[:, hd, :], la[:, j, hd:hd + 1].to_broadcast([P, P]), c.upto[:],
                                      start=True, stop=True)
                    mm.then_inc(cr_full, 1)

                def x_to_tokens(n, j):
                    pe.wait_ge(xt_ready, n * 2 + 2)
                    if j == 0:
                        pe.wait_ge(out_ready, n * TM)
                    else:
                        pe.wait_ge(xdt_ready, n * TM + j)
                    for m in range(CI):
                        mm = t.matmul(heads(p_x)[:, m, :], xt[:, m, j * P:(j + 1) * P], c.ident[:],
                                      is_transpose=True, start=True, stop=True)
                    mm.then_inc(xtr_full, 1)

                def y_product(n, j):
                    pe.wait_ge(xdt_ready, n * TM + j + 1)
                    pe.wait_ge(decay_ready, n * TM + j + 1)
                    pe.wait_ge(cdec_ready, n * TM + j + 1)
                    pe.wait_ge(state_ready, n * TM + j + 1)
                    wait(pe, y_read, n * TM + j)
                    for hd in range(NH):
                        out = heads(p_y)[:, hd, :]
                        t.matmul(out, xdt[j][:, hd, :], decay[j][:, hd, :], start=True, stop=False)
                        mm = t.matmul(out, state[:, hd, :], cdec[j][:, hd, :], start=False, stop=True)
                    mm.then_inc(y_full, 1)

                def state_product(n, j):
                    pe.wait_ge(xs_ready, n * TM + j + 1)
                    if is_(n, NM - 1) and j == 0:
                        pe.wait_ge(diff_ready, (n * TM + TM) * NH)
                    elif j == 0:
                        pe.wait_ge(ht_ready, (n + 1) * 2 + 2)
                    else:
                        pe.wait_ge(state_ready, n * TM + j + 1)
                    for b in range(2):
                        mm = t.matmul(p_cr[:, b, :], btok[:, j, :],
                                      xs[:, :, :].rearrange("p h q -> p (h q)")[:, b * 512:(b + 1) * 512],
                                      start=True, stop=True)
                    mm.then_inc(s_full, 1)

                def out_product(n, j):
                    pe.wait_ge(y_ready, n * TM + j + 1)
                    if j == 0:
                        pe.wait_ge(xdt_ready, n * TM + TM)
                    for m in range(CI):
                        mm = three(p_x[:, j, :], y_hi[:, m, :], y_lo[:, m, :], wo_hi[:, m, :], wo_lo[:, m, :],
                                   m == 0, m == CI - 1)
                    mm.then_inc(out_full, 1)

                def head(n):
                    pe.wait_ge(ht_ready, n * 2 + 2)
                    project(n, J_DT, DT0, NH)
                    project(n, J_C, C0)
                    project(n, J_B, B0)

                def block_(n, it, u):
                    ssm_part = lambda m: project(n, J_SSM[m], SSM0 + m * P)
                    gate_part = lambda m: project(n, J_GATE[m], GATE0 + m * P)
                    to_tokens(n)
                    ssm_part(0)
                    ssm_part(1)
                    if not is_(n, 0):
                        out_product(n - 1, 1)
                    cumulate(n)
                    ssm_part(2)
                    b_by_c(n)
                    spread(n, 0)
                    for m in range(3, 6):
                        ssm_part(m)
                    spread(n, 1)
                    for m in range(6, CI):
                        ssm_part(m)
                    for m in range(6):
                        gate_part(m)
                    x_to_tokens(n, 0)
                    gate_part(6)
                    gate_part(7)
                    if not is_(n, NM - 1):
                        turn(n + 1)
                    x_to_tokens(n, 1)
                    y_product(n, 0)
                    state_product(n, 0)
                    if not is_(n, NM - 1):
                        head(n + 1)
                    y_product(n, 1)
                    state_product(n, 1)
                    out_product(n, 0)

                turn(0)
                pe.wait_ge(w_lo_done, N_PIECES)
                head(0)
                ends_split(t, NM // 2, pairs(block_))
                out_product(NM - 1, 1)

            @block.vector
            def _(dve):
                v = nc.vector
                steps = [0, 0]

                def link(ins):
                    steps[1] += 1
                    ins.then_inc(dve_step, 1)
                    dve.wait_ge(dve_step, steps[0] + steps[1])

                def link_apart(ins):
                    steps[1] += 1
                    ins.then_inc(dve_step, 1)
                    wait_apart(c, v, (dve_step, steps[0] + steps[1]))

                v.memset(state[:], 0.0).then_inc(state_ready, 1)
                for i in range(N_PIECES):
                    dve.wait_ge(w_hi_done, i + 1)
                    _, cols, hi, lo, scale = piece(i)
                    part = stage[i % 3][:, 0:cols]
                    if scale is not None:
                        v.scalar_tensor_tensor(lo, part, scale, hi.bitcast(F32), ALU.mult, ALU.subtract).then_inc(w_lo_done, 1)
                    else:
                        v.tensor_tensor(lo, part, hi.bitcast(F32), ALU.subtract).then_inc(w_lo_done, 1)
                dve.wait_ge(a_exp, 1)
                v.tensor_scalar(a_neg[:], a_neg[:], -1.0, None, ALU.mult).then_inc(set_up, 1)
                dve.wait_ge(w_lo_done, N_PIECES)
                v.memset(ssm[:], 0.0).then_inc(halo_ready, 1)

                def norm_stats(n, it, u):
                    dve.wait_ge(x_loaded[u], it * 16 + 16)
                    for j in range(TM):
                        ins_ = v.bn_stats(stats[:, j, :], x[u][:, j, :])
                    link_apart(ins_)
                    for j in range(TM):
                        ins_ = v.bn_aggr(mv[:, j, :], stats[:, j, :])
                    link(ins_)
                    v.tensor_scalar(var2[:, 0, :], mv[:, :, 1], LN_EPS, None, ALU.add)
                    v.tensor_scalar(var2[:, 1, :], mv[:, :, 1], 1.0 + RMS_EPS, RMS_EPS * LN_EPS,
                                    ALU.mult, ALU.add).then_inc(var_ready, 1)

                def norm_apply(n, it, u):
                    dve.wait_ge(inv_ready, n + 1)
                    dve.wait_ge(ht_ready, n * 2)
                    for j in range(TM):
                        v.tensor_scalar(h[:, j, :], x[u][:, j, :], mv[:, j, 0:1], inv2[:, 1, j:j + 1],
                                        ALU.subtract, ALU.mult).then_inc(h_ready, 1)
                    v.tensor_tensor(mean_inv[:], mv[:, :, 0], inv2[:, 0, :], ALU.mult)
                    link(v.tensor_scalar(one_inv[:], inv2[:, 0, :], 1.0, None, ALU.add))
                    dve.wait_ge(h_ready, n * TM + TM)
                    for j in range(TM):
                        ins_ = v.tensor_scalar(x[u][:, j, :], x[u][:, j, :], one_inv[:, j:j + 1], mean_inv[:, j:j + 1],
                                               ALU.mult, ALU.subtract)
                    link(ins_)

                def turned(n):
                    for r in range(2):
                        dve.wait_ge(ht_hi_ready, n * 2 + r + 1)
                        v.tensor_tensor(ht_lo[:, 2 * r:2 * r + 2, :], p_cr[:, r, :].rearrange("p (k t) -> p k t", k=2),
                                        ht_hi[:, 2 * r:2 * r + 2, :].bitcast(F32), ALU.subtract).then_inc(ht_ready, 1)

                def time_steps(n):
                    dve.wait_ge(ab_free, n * JOBS + J_TOK + 1)
                    link(v.tensor_tensor(dtv[:], dtraw.rearrange("p (j h) -> p j h", j=TM),
                                         dtb[:].unsqueeze(1).to_broadcast([P, TM, NH]), ALU.add))
                    v.scalar_tensor_tensor(nabs[:], dtv[:], -1.0, dtv[:], ALU.mult, ALU.min).then_inc(nabs_ready, 1)
                    dve.wait_ge(soft_ready, n + 1)
                    dve.wait_ge(cr_full, n * TM)
                    link(v.scalar_tensor_tensor(dt[:], dtv[:], 0.0, nabs[:], ALU.max, ALU.add))
                    v.tensor_tensor(la[:], dt[:], a_neg[:].unsqueeze(1).to_broadcast([P, TM, NH]),
                                    ALU.mult).then_inc(la_ready, 1)

                def ends(n):
                    dve.wait_ge(ab_free, n * JOBS + J_CUM + 1)
                    dve.wait_ge(xs_ready, n * TM)
                    v.tensor_tensor(to_end[:], cum[:, 1, :, :], cum[:, 0, :, :], ALU.subtract).then_inc(to_end_ready, 1)

                def mask_cb(n):
                    dve.wait_ge(ab_free, n * JOBS + J_CB + 1)
                    link(v.tensor_tensor(cb[:], cb[:], c.upto[:].unsqueeze(1).to_broadcast([P, TM, P]), ALU.mult))

                def differences(n, j):
                    dve.wait_ge(cdec_exp, n * TM + j + 1)
                    dve.wait_ge(y_full, n * TM)
                    for hd in range(NH):
                        v.tensor_scalar(decay[j][:, hd, :], heads(p_cr)[:, hd, :], cum[:, 0, j, hd:hd + 1], 0.0,
                                        ALU.subtract, ALU.min).then_inc(diff_ready, 1)

                def by_cb(n, j):
                    dve.wait_ge(decay_exp, n * TM + j + 1)
                    v.tensor_tensor(decay[j][:], decay[j][:], cb[:, j, :].unsqueeze(1).to_broadcast([P, NH, P]),
                                    ALU.mult).then_inc(decay_ready, 1)

                def convolve(n, m):
                    dve.wait_ge(ab_free, n * JOBS + J_SSM[m] + 1)
                    for i in range(HALO):
                        ins_ = v.scalar_tensor_tensor(xt[:, m, :], ssm[:, m, i:i + BM], convw[:, m, i:i + 1],
                                                      xt[:, m, :], ALU.mult, ALU.add)
                        if i < HALO - 1:
                            link(ins_)
                    ins_.then_inc(conv_ready, 1)

                def times_dt(n, j):
                    dve.wait_ge(xtr_full, n * TM + j + 1)
                    wait(dve, y_full, n * TM)
                    wait(dve, xs_ready, n * TM)
                    v.tensor_tensor(xdt[j][:], heads(p_x), dt[:, j, :].unsqueeze(2).to_broadcast([P, NH, HP]),
                                    ALU.mult).then_inc(xdt_ready, 1)

                def skip_part(n, j):
                    tokens = slice(j * P, (j + 1) * P)
                    dve.wait_ge(y_full, n * TM + j + 1)
                    for m in range(CI):
                        ins_ = v.scalar_tensor_tensor(xt[:, m, tokens], xt[:, m, tokens], dskip[:, m:m + 1],
                                                      heads(p_y)[:, m, :], ALU.mult, ALU.add)
                    ins_.then_inc(y_read, 1)

                def gated(n, j):
                    tokens = slice(j * P, (j + 1) * P)
                    dve.wait_ge(y_read, n * TM + j + 1)
                    dve.wait_ge(gate_ready, n + 1)
                    v.tensor_tensor(xt[:, :, tokens], xt[:, :, tokens], gate[:, :, tokens], ALU.mult).then_inc(y_gated, 1)

                def halves(n, j):
                    dve.wait_ge(y_hi_ready, n * TM + j + 1)
                    v.tensor_tensor(y_lo[:], xt[:, :, j * P:(j + 1) * P], y_hi[:].bitcast(F32),
                                    ALU.subtract).then_inc(y_ready, 1)

                def add_state(n, j):
                    dve.wait_ge(s_full, n * TM + j + 1)
                    dve.wait_ge(state_dec_ready, n * TM + j + 1)
                    v.tensor_tensor(state[:], state_dec[:], heads(p_cr), ALU.add).then_inc(state_ready, 1)

                def add_out(n, u, j):
                    dve.wait_ge(out_full, n * TM + j + 1)
                    v.tensor_tensor(x[u][:, j, :], p_x[:, j, :], x[u][:, j, :], ALU.add).then_inc(out_ready, 1)

                norm_stats(0, 0, 0)
                norm_apply(0, 0, 0)
                turned(0)
                HEAD = steps[1]

                def block_(n, it, u):
                    nn, nit, nu = n + 1, (it if u == 0 else it + 1), 1 - u
                    more = not is_(n, NM - 1)
                    steps[0], steps[1] = n * BODY + HEAD, 0
                    time_steps(n)
                    if not is_(n, 0):
                        add_out(n - 1, 1 - u, 0)
                    convolve(n, 0)
                    convolve(n, 1)
                    if not is_(n, 0):
                        add_out(n - 1, 1 - u, 1)
                    ends(n)
                    convolve(n, 2)
                    mask_cb(n)
                    differences(n, 0)
                    convolve(n, 3)
                    by_cb(n, 0)
                    convolve(n, 4)
                    convolve(n, 5)
                    differences(n, 1)
                    if more:
                        norm_stats(nn, nit, nu)
                    by_cb(n, 1)
                    convolve(n, 6)
                    convolve(n, 7)
                    if more:
                        dve.wait_ge(conv_ready, n * CI + CI)
                        v.tensor_scalar(ssm[:, :, 0:HALO], ssm[:, :, BM:BM + HALO], c.keep[:, bass.ds(nn, 1)], None,
                                        ALU.mult).then_inc(halo_ready, 1)
                        norm_apply(nn, nit, nu)
                    times_dt(n, 0)
                    if more:
                        turned(nn)
                    times_dt(n, 1)
                    skip_part(n, 0)
                    gated(n, 0)
                    add_state(n, 0)
                    halves(n, 0)
                    skip_part(n, 1)
                    gated(n, 1)
                    add_state(n, 1)
                    halves(n, 1)
                    if more:
                        assert steps[1] == BODY, steps
                BODY = HEAD + 3 + 2 * CI
                ends_split(v, NM // 2, pairs(block_))
                add_out(NM - 1, 1, 0)
                add_out(NM - 1, 1, 1)


def build(nc, ins, out):
    with ExitStack() as ctx:
        def sb(name, shape, dt=F32):
            return ctx.enter_context(nc.sbuf_tensor(name, shape, dt))

        c = Names()
        c.ones, c.ident, c.upto = sb("ones", [P, P]), sb("ident", [P, P]), sb("upto", [P, P])
        c.before, c.ones_bf = sb("before", [P, P], BF16), sb("ones_bf", [P, P], BF16)
        c.expert_no, c.neg_half = sb("expert_no", [P, E]), sb("neg_half", [P, 8])
        c.keep, c.cut = sb("keep", [P, NM + 1]), sb("cut", [P, NM])
        c.fold, c.token_no = sb("fold", [P, E]), sb("token_no", [P, TILES])
        c.slot_no, c.spare_row = sb("slot_no", [P, PAIRS]), sb("spare_row", [P, 1])
        after_ffn = nc.dram_tensor("after_ffn", (T + P, D), F32).ap()
        after_mamba = nc.dram_tensor("after_mamba", (T, D), F32).ap()
        xg = nc.dram_tensor("slot_rows", (SLOTS, ROW), F32).ap()
        ffn = (ins["shw"], ins["routw"], ins["routb"])

        s = lambda name: ctx.enter_context(nc.semaphore(name))
        make_constants(nc, c, s)
        with Phase(nc) as s:
            route_and_shared(nc, "a", c, s, ins["x"], after_ffn, xg, *ffn, 0, True)
        with Phase(nc) as s:
            experts(nc, "a", c, s, xg, ins["ew"], after_ffn, 0)
        with Phase(nc) as s:
            mamba(nc, c, s, after_ffn, after_mamba, ins)
        with Phase(nc) as s:
            route_and_shared(nc, "b", c, s, after_mamba, out, xg, *ffn, T, False)
        with Phase(nc) as s:
            experts(nc, "b", c, s, xg, ins["ew"], out, T)


def layouts(np, inputs):
    g = {k: np.asarray(v) for k, v in inputs.items()}

    def by_slice(w, n):
        return w.reshape(n, P, -1).transpose(1, 0, 2).reshape(P, -1)

    gate = g["L0_ffn_sh_gate_w"].reshape(FS, D).T
    up = g["L0_ffn_sh_up_w"].reshape(FS, D).T
    gate_up = np.stack([w.reshape(KD, P, CF, P).transpose(1, 2, 0, 3) for w in (gate, up)], axis=2).reshape(P, -1)
    down = g["L0_ffn_sh_down_w"].transpose(0, 2, 1).reshape(FS, D)
    eg = g["L0_ffn_gate_w"].transpose(0, 2, 1).reshape(E, KD, P, F).transpose(0, 2, 1, 3)
    eu = g["L0_ffn_up_w"].transpose(0, 2, 1).reshape(E, KD, P, F).transpose(0, 2, 1, 3)
    gu = np.stack([eg, eu], axis=3).reshape(E, P, KD * 2 * F)
    ed = g["L0_ffn_down_w"].transpose(0, 2, 1)
    ew = np.concatenate([gu, ed], axis=2).reshape(PAIRS, 2, P, EW).transpose(0, 2, 1, 3)
    arrays = {
        "x": g["L0_attn_x"].reshape(T, D),
        "shw": np.concatenate([gate_up, by_slice(down, CF)], axis=1),
        "routw": by_slice(g["L0_ffn_router_w"].T, KD),
        "routb": g["L0_ffn_router_bias"].reshape(1, E),
        "ew": ew,
        "winp": by_slice(g["L0_attn_in_proj_w"], KD),
        "wout": by_slice(g["L0_attn_out_proj_w"], CI),
        "nscale": g["L0_attn_norm_scale"].reshape(KD, P).T,
        "convw": by_slice(g["L0_attn_conv_weight"].T, CI),
        "convb": g["L0_attn_conv_bias"].reshape(CI, P).T,
        "dskip": g["L0_attn_D"].reshape(CI, P).T,
        "dtb": g["L0_attn_dt_bias"].reshape(1, NH),
        "alog": g["L0_attn_A_log"].reshape(1, NH),
    }
    return {k: np.ascontiguousarray(a) for k, a in arrays.items()}


def kernel(**inputs):
    import numpy as np
    import concourse.bacc as bacc
    from concourse.bass_utils import run_bass_kernel_spmd

    arrays = {f"in_{name}": a for name, a in layouts(np, inputs).items()}
    nc = bacc.Bacc("TRN2", target_bir_lowering=False, num_devices=1)
    ins = {name[3:]: nc.dram_tensor(name, a.shape, mybir.dt.from_np(a.dtype), kind="ExternalInput").ap()
           for name, a in arrays.items()}
    out = nc.dram_tensor("out", (T + P, D), F32, kind="ExternalOutput").ap()
    build(nc, ins, out)
    result = run_bass_kernel_spmd(nc, [arrays], core_ids=[0])
    return result.results[0]["out"][0:T].reshape(BATCH, SEQ, D)
```
